# Optimizing a Trainium2 kernel written in Bass

```python
import numpy as np
import jax
import jax.numpy as jnp

def _softmax(x, axis=-1):
    return jax.nn.softmax(x, axis=axis)

def _gelu(x):
    return jax.nn.gelu(x, approximate=True)

def _silu(x):
    return jax.nn.silu(x)

def _sigmoid(x):
    return jax.nn.sigmoid(x)

def _layernorm(x, axis=-1, eps=1e-05):
    m = jnp.mean(x, axis=axis, keepdims=True)
    v = jnp.var(x, axis=axis, keepdims=True)
    return (x - m) / jnp.sqrt(v + eps)

def _scatter_add(tgt, idx, src, axis=0):
    return tgt.at[idx].add(src)

def _segment_sum(src, seg, n):
    return jax.ops.segment_sum(src, seg, n)
kernel_name = 'mk_perceiver_d1_seqx_r4_43f408'

def setup_inputs(seed: int=0):
    np.random.seed(seed)
    _w = jnp.asarray

    def _rec_inputs():
        import jax
        import jax.numpy as jnp
        _rk = jax.random.key(seed)
        x = -0.0002928 + 1 * jax.random.normal(jax.random.fold_in(_rk, 1), (8, 64, 256), jnp.float32)
        _lenS = 64 - jax.random.randint(jax.random.fold_in(_rk, 7), (8,), 0, max(1, 64 // 4) + 1, jnp.int32)
        _lenS2 = 1601 - jax.random.randint(jax.random.fold_in(_rk, 8), (8,), 0, max(1, 1601 // 4) + 1, jnp.int32)
        _ctx_1024P = jax.random.normal(jax.random.fold_in(_rk, 11), (8, 16, 256), jnp.float32)
        _ctx_1024c = jax.random.dirichlet(jax.random.fold_in(_rk, 511), 0.3 * jnp.ones((16,), jnp.float32), (8, 1601))
        _ctx_1024t = jnp.einsum('bsk,bkd->bsd', _ctx_1024c, _ctx_1024P)
        _ctx_1024t = _ctx_1024t * jax.lax.rsqrt(jnp.mean(jnp.square(_ctx_1024t)) + 1e-12) * 0.953939
        ctx_1024 = -1.39393e-06 + 0.999914 * (_ctx_1024t + 0.3 * jax.random.normal(jax.random.fold_in(_rk, 611), (8, 1601, 256), jnp.float32))
        return (x, ctx_1024)
    x, ctx_1024 = _rec_inputs()

    def _L0_xattn_setup():
        import jax, jax.numpy as jnp
        import numpy as np
        D_MODEL = 256
        NUM_HEADS = 16
        D_K = D_MODEL // NUM_HEADS

        def _split_heads(x):
            B, S, _ = x.shape
            return x.reshape(B, S, NUM_HEADS, D_K).transpose(0, 2, 1, 3)
        key = jax.random.key(seed)
        ks = jax.random.split(key, 11)
        B, S = (2, 512)
        scale = 1.0 / np.sqrt(D_MODEL)
        inp = {'q': jax.random.normal(ks[0], (B, S, D_MODEL), jnp.float32), 'k': jax.random.normal(ks[1], (B, S, D_MODEL), jnp.float32), 'v': jax.random.normal(ks[2], (B, S, D_MODEL), jnp.float32), 'Wq': jax.random.normal(ks[3], (D_MODEL, D_MODEL), jnp.float32) * scale, 'bq': jnp.zeros((D_MODEL,), jnp.float32), 'Wk': jax.random.normal(ks[4], (D_MODEL, D_MODEL), jnp.float32) * scale, 'bk': jnp.zeros((D_MODEL,), jnp.float32), 'Wv': jax.random.normal(ks[5], (D_MODEL, D_MODEL), jnp.float32) * scale, 'bv': jnp.zeros((D_MODEL,), jnp.float32), 'Wo': jax.random.normal(ks[6], (D_MODEL, D_MODEL), jnp.float32) * scale, 'bo': jnp.zeros((D_MODEL,), jnp.float32)}
        return inp
    _L0_xattn_all = _L0_xattn_setup()
    _L0_xattn_in = {k: v for k, v in _L0_xattn_all.items() if k in ('Wq', 'bq', 'Wk', 'bk', 'Wv', 'bv', 'Wo', 'bo')}
    del _L0_xattn_all

    def _L0_attn_setup():
        import jax, jax.numpy as jnp
        import numpy as np
        D = 256
        H = 16
        KVH = 4
        HD = D // H
        LAT = 64
        WIN = 64
        B, S = (1, 512)
        BASE_G, BASE_L = (1000000.0, 10000.0)
        EPS = 1e-06

        def rmsnorm(x, w):
            return x * jax.lax.rsqrt(jnp.mean(x * x, axis=-1, keepdims=True) + EPS) * w

        def qk_norm(x):
            return x * jax.lax.rsqrt(jnp.mean(x * x, axis=-1, keepdims=True) + EPS)

        def rope(x, base):
            s, hd = (x.shape[-2], x.shape[-1])
            inv_freq = 1.0 / base ** (jnp.arange(0, hd, 2, dtype=jnp.float32) / hd)
            freqs = jnp.arange(s, dtype=jnp.float32)[:, None] * inv_freq[None, :]
            cos, sin = (jnp.cos(freqs), jnp.sin(freqs))
            xe, xo = (x[..., ::2], x[..., 1::2])
            out = jnp.stack([xe * cos - xo * sin, xe * sin + xo * cos], axis=-1)
            return out.reshape(x.shape)

        def split_heads(x, n_heads):
            b, s, _ = x.shape
            return x.reshape(b, s, n_heads, HD).transpose(0, 2, 1, 3)

        def repeat_kv(x):
            return jnp.repeat(x, H // KVH, axis=1)

        def sdpa(q, k, v, mask):
            scores = jnp.einsum('bhqd,bhkd->bhqk', q, k) / np.sqrt(HD).astype(np.float32)
            scores = jnp.where(mask, scores, jnp.float32(-1e+30))
            probs = jax.nn.softmax(scores, axis=-1)
            return jnp.einsum('bhqk,bhkd->bhqd', probs, v)

        def merge_heads(x):
            b, h, s, hd = x.shape
            return x.transpose(0, 2, 1, 3).reshape(b, s, h * hd)

        def global_latent_attn(x, wq, w_kv_down, w_k_up, w_v_up, wo):
            q = split_heads(x @ wq, H)
            latent = x @ w_kv_down
            k = split_heads(latent @ w_k_up, KVH)
            v = split_heads(latent @ w_v_up, KVH)
            q, k = (rope(q, BASE_G), rope(k, BASE_G))
            q, k = (qk_norm(q), qk_norm(k))
            k, v = (repeat_kv(k), repeat_kv(v))
            i = jnp.arange(x.shape[1])
            causal = i[:, None] >= i[None, :]
            return merge_heads(sdpa(q, k, v, causal)) @ wo

        def local_gqa_attn(x, wq, wk, wv, wo):
            q = split_heads(x @ wq, H)
            k = split_heads(x @ wk, KVH)
            v = split_heads(x @ wv, KVH)
            q, k = (rope(q, BASE_L), rope(k, BASE_L))
            q, k = (qk_norm(q), qk_norm(k))
            k, v = (repeat_kv(k), repeat_kv(v))
            i = jnp.arange(x.shape[1])
            diff = i[:, None] - i[None, :]
            mask = (diff >= 0) & (diff < WIN)
            return merge_heads(sdpa(q, k, v, mask)) @ wo
        key = jax.random.key(seed)
        ks = jax.random.split(key, 12)
        std = 0.02
        return {'hidden': jax.random.normal(ks[0], (B, S, D), dtype=jnp.float32), 'norm1_w': jnp.ones((D,), jnp.float32), 'norm2_w': jnp.ones((D,), jnp.float32), 'g_wq': jax.random.normal(ks[1], (D, H * HD), jnp.float32) * std, 'g_kv_down': jax.random.normal(ks[2], (D, LAT), jnp.float32) * std, 'g_k_up': jax.random.normal(ks[3], (LAT, KVH * HD), jnp.float32) * std, 'g_v_up': jax.random.normal(ks[4], (LAT, KVH * HD), jnp.float32) * std, 'g_wo': jax.random.normal(ks[5], (D, D), jnp.float32) * std, 'l_wq': jax.random.normal(ks[6], (D, H * HD), jnp.float32) * std, 'l_wk': jax.random.normal(ks[7], (D, KVH * HD), jnp.float32) * std, 'l_wv': jax.random.normal(ks[8], (D, KVH * HD), jnp.float32) * std, 'l_wo': jax.random.normal(ks[9], (D, D), jnp.float32) * std}
    _L0_attn_all = _L0_attn_setup()
    _L0_attn_in = {k: v for k, v in _L0_attn_all.items() if k in ('norm1_w', 'norm2_w', 'g_wq', 'g_kv_down', 'g_k_up', 'g_v_up', 'g_wo', 'l_wq', 'l_wk', 'l_wv', 'l_wo')}
    del _L0_attn_all

    def _L0_ffn_setup():
        import jax, jax.numpy as jnp
        import numpy as np
        B, S, D, E = (2, 512, 256, 8)
        key = jax.random.key(seed)
        ks = jax.random.split(key, 5)
        x = jax.random.normal(ks[0], (B, S, D), dtype=jnp.float32)
        router_w = jax.random.normal(ks[1], (E, D), dtype=jnp.float32) * 0.02
        router_b = jnp.zeros((E,), dtype=jnp.float32)
        expert_w = jax.random.normal(ks[2], (E, D, D), dtype=jnp.float32) * 0.02
        expert_b = jnp.zeros((E, D), dtype=jnp.float32)
        return {'x': x, 'router_w': router_w, 'router_b': router_b, 'expert_w': expert_w, 'expert_b': expert_b}
    _L0_ffn_all = _L0_ffn_setup()
    _L0_ffn_in = {k: v for k, v in _L0_ffn_all.items() if k in ('router_w', 'router_b', 'expert_w', 'expert_b')}
    del _L0_ffn_all
    return {'x': x, 'ctx_1024': ctx_1024, 'L0_xattn_Wq': _L0_xattn_in['Wq'], 'L0_xattn_bq': _L0_xattn_in['bq'], 'L0_xattn_Wk': _L0_xattn_in['Wk'], 'L0_xattn_bk': _L0_xattn_in['bk'], 'L0_xattn_Wv': _L0_xattn_in['Wv'], 'L0_xattn_bv': _L0_xattn_in['bv'], 'L0_xattn_Wo': _L0_xattn_in['Wo'], 'L0_xattn_bo': _L0_xattn_in['bo'], 'L0_attn_norm1_w': _L0_attn_in['norm1_w'], 'L0_attn_norm2_w': _L0_attn_in['norm2_w'], 'L0_attn_g_wq': _L0_attn_in['g_wq'], 'L0_attn_g_kv_down': _L0_attn_in['g_kv_down'], 'L0_attn_g_k_up': _L0_attn_in['g_k_up'], 'L0_attn_g_v_up': _L0_attn_in['g_v_up'], 'L0_attn_g_wo': _L0_attn_in['g_wo'], 'L0_attn_l_wq': _L0_attn_in['l_wq'], 'L0_attn_l_wk': _L0_attn_in['l_wk'], 'L0_attn_l_wv': _L0_attn_in['l_wv'], 'L0_attn_l_wo': _L0_attn_in['l_wo'], 'L0_ffn_router_w': _L0_ffn_in['router_w'], 'L0_ffn_router_b': _L0_ffn_in['router_b'], 'L0_ffn_expert_w': _L0_ffn_in['expert_w'], 'L0_ffn_expert_b': _L0_ffn_in['expert_b']}

def reference(x, ctx_1024, L0_xattn_Wq, L0_xattn_bq, L0_xattn_Wk, L0_xattn_bk, L0_xattn_Wv, L0_xattn_bv, L0_xattn_Wo, L0_xattn_bo, L0_attn_norm1_w, L0_attn_norm2_w, L0_attn_g_wq, L0_attn_g_kv_down, L0_attn_g_k_up, L0_attn_g_v_up, L0_attn_g_wo, L0_attn_l_wq, L0_attn_l_wk, L0_attn_l_wv, L0_attn_l_wo, L0_ffn_router_w, L0_ffn_router_b, L0_ffn_expert_w, L0_ffn_expert_b):
    import jax
    import jax.numpy as jnp

    def _L0_xattn_ref(q, k, v, Wq, bq, Wk, bk, Wv, bv, Wo, bo):
        import jax, jax.numpy as jnp
        import numpy as np
        D_MODEL = 256
        NUM_HEADS = 16
        D_K = D_MODEL // NUM_HEADS

        def _split_heads(x):
            B, S, _ = x.shape
            return x.reshape(B, S, NUM_HEADS, D_K).transpose(0, 2, 1, 3)
        B, S, _ = q.shape
        qh = _split_heads(q @ Wq + bq)
        kh = _split_heads(k @ Wk + bk)
        vh = _split_heads(v @ Wv + bv)
        scores = jnp.einsum('bhsd,bhtd->bhst', qh, kh) / np.sqrt(D_K)
        attn = jax.nn.softmax(scores, axis=-1)
        out = jnp.einsum('bhst,bhtd->bhsd', attn, vh)
        out = out.transpose(0, 2, 1, 3).reshape(B, S, D_MODEL)
        return out @ Wo + bo

    def _L0_attn_ref(hidden, norm1_w, norm2_w, g_wq, g_kv_down, g_k_up, g_v_up, g_wo, l_wq, l_wk, l_wv, l_wo):
        import jax, jax.numpy as jnp
        import numpy as np
        D = 256
        H = 16
        KVH = 4
        HD = D // H
        LAT = 64
        WIN = 64
        B, S = (1, 512)
        BASE_G, BASE_L = (1000000.0, 10000.0)
        EPS = 1e-06

        def rmsnorm(x, w):
            return x * jax.lax.rsqrt(jnp.mean(x * x, axis=-1, keepdims=True) + EPS) * w

        def qk_norm(x):
            return x * jax.lax.rsqrt(jnp.mean(x * x, axis=-1, keepdims=True) + EPS)

        def rope(x, base):
            s, hd = (x.shape[-2], x.shape[-1])
            inv_freq = 1.0 / base ** (jnp.arange(0, hd, 2, dtype=jnp.float32) / hd)
            freqs = jnp.arange(s, dtype=jnp.float32)[:, None] * inv_freq[None, :]
            cos, sin = (jnp.cos(freqs), jnp.sin(freqs))
            xe, xo = (x[..., ::2], x[..., 1::2])
            out = jnp.stack([xe * cos - xo * sin, xe * sin + xo * cos], axis=-1)
            return out.reshape(x.shape)

        def split_heads(x, n_heads):
            b, s, _ = x.shape
            return x.reshape(b, s, n_heads, HD).transpose(0, 2, 1, 3)

        def repeat_kv(x):
            return jnp.repeat(x, H // KVH, axis=1)

        def sdpa(q, k, v, mask):
            scores = jnp.einsum('bhqd,bhkd->bhqk', q, k) / np.sqrt(HD).astype(np.float32)
            scores = jnp.where(mask, scores, jnp.float32(-1e+30))
            probs = jax.nn.softmax(scores, axis=-1)
            return jnp.einsum('bhqk,bhkd->bhqd', probs, v)

        def merge_heads(x):
            b, h, s, hd = x.shape
            return x.transpose(0, 2, 1, 3).reshape(b, s, h * hd)

        def global_latent_attn(x, wq, w_kv_down, w_k_up, w_v_up, wo):
            q = split_heads(x @ wq, H)
            latent = x @ w_kv_down
            k = split_heads(latent @ w_k_up, KVH)
            v = split_heads(latent @ w_v_up, KVH)
            q, k = (rope(q, BASE_G), rope(k, BASE_G))
            q, k = (qk_norm(q), qk_norm(k))
            k, v = (repeat_kv(k), repeat_kv(v))
            i = jnp.arange(x.shape[1])
            causal = i[:, None] >= i[None, :]
            return merge_heads(sdpa(q, k, v, causal)) @ wo

        def local_gqa_attn(x, wq, wk, wv, wo):
            q = split_heads(x @ wq, H)
            k = split_heads(x @ wk, KVH)
            v = split_heads(x @ wv, KVH)
            q, k = (rope(q, BASE_L), rope(k, BASE_L))
            q, k = (qk_norm(q), qk_norm(k))
            k, v = (repeat_kv(k), repeat_kv(v))
            i = jnp.arange(x.shape[1])
            diff = i[:, None] - i[None, :]
            mask = (diff >= 0) & (diff < WIN)
            return merge_heads(sdpa(q, k, v, mask)) @ wo
        x = hidden
        x = x + global_latent_attn(rmsnorm(x, norm1_w), g_wq, g_kv_down, g_k_up, g_v_up, g_wo)
        x = x + local_gqa_attn(rmsnorm(x, norm2_w), l_wq, l_wk, l_wv, l_wo)
        return x

    def _L0_ffn_ref(x, router_w, router_b, expert_w, expert_b):
        import jax, jax.numpy as jnp
        import numpy as np
        B, S, D, E = (2, 512, 256, 8)
        logits = jnp.einsum('bsd,ed->bse', x, router_w) + router_b
        probs = jax.nn.softmax(logits, axis=-1)
        weights = jnp.max(probs, axis=-1)
        top1 = jnp.argmax(probs, axis=-1)
        y_all = jnp.einsum('bsd,eod->bseo', x, expert_w) + expert_b
        y = jnp.take_along_axis(y_all, top1[:, :, None, None], axis=2)[:, :, 0, :]
        out = y * weights[:, :, None]
        return out
    x = x + _L0_xattn_ref(_layernorm(x, axis=-1), ctx_1024, ctx_1024, L0_xattn_Wq, L0_xattn_bq, L0_xattn_Wk, L0_xattn_bk, L0_xattn_Wv, L0_xattn_bv, L0_xattn_Wo, L0_xattn_bo)
    x = x + _L0_attn_ref(_layernorm(x, axis=-1), L0_attn_norm1_w, L0_attn_norm2_w, L0_attn_g_wq, L0_attn_g_kv_down, L0_attn_g_k_up, L0_attn_g_v_up, L0_attn_g_wo, L0_attn_l_wq, L0_attn_l_wk, L0_attn_l_wv, L0_attn_l_wo)
    x = x + _L0_ffn_ref(_layernorm(x, axis=-1), L0_ffn_router_w, L0_ffn_router_b, L0_ffn_expert_w, L0_ffn_expert_b)
    return x

_drawn_inputs = setup_inputs


def setup_inputs(seed=0):
    import zlib

    import numpy as np

    out = dict(_drawn_inputs(seed))
    spreads = {'L0_xattn_bq': (0.0, 0.388),
     'L0_xattn_bk': (0.0, 2.0),
     'L0_xattn_bv': (0.0, 0.1),
     'L0_xattn_bo': (0.0, 0.1),
     'L0_attn_norm1_w': (1.0, 0.6),
     'L0_attn_norm2_w': (1.0, 0.6),
     'L0_ffn_router_b': (0.0, 1.394),
     'L0_ffn_expert_b': (0.0, 2.0)}
    factors = {'L0_attn_g_wq': 8.0,
     'L0_attn_g_kv_down': 8.0,
     'L0_attn_g_k_up': 8.0,
     'L0_attn_g_v_up': 8.0,
     'L0_attn_g_wo': 8.0,
     'L0_attn_l_wq': 45.592,
     'L0_attn_l_wk': 45.928,
     'L0_attn_l_wv': 2.829,
     'L0_attn_l_wo': 2.838,
     'L0_ffn_expert_w': 5.236}
    for name, (base, spread) in spreads.items():
        noise = np.random.default_rng([zlib.crc32(name.encode()), seed]).standard_normal(out[name].shape)
        drawn = base * np.exp(spread * noise) if base else spread * noise
        out[name] = jnp.asarray(drawn.astype(out[name].dtype))
    for name, factor in factors.items():
        out[name] = (out[name] * factor).astype(out[name].dtype)
    return out
```

```python
from contextlib import ExitStack

import concourse.bass as bass
import numpy as np
from concourse import mybir

F32 = mybir.dt.float32
F32R = mybir.dt.float32r
ALU = mybir.AluOpType
ACT = mybir.ActivationFunctionType
AX = mybir.AxisListType

P = 128
B, NQ, D = 8, 64, 256
T = 1601
H, DH = 16, 16
DC = D // P
HC = H // DC
PAIRS = HC // 2
TP = T + 1
NT = -(-T // P)
TLAST = T - (NT - 1) * P
NCH = 4
CH = 402
VW = DH + 1
COLS = HC * NQ
TT = B * NQ // P
LN_EPS = 1e-5
RMS_EPS = 1e-6
KV, LAT = 4, 64
E = 8

POS = 2 * NT
AHEAD = [[] for _ in range(POS)]
for _n in range(NCH):
    AHEAD[_n].append(("K", 0, _n))
AHEAD[4].append(("OUT",))
for _n, _k in enumerate((6, 7, 9, 10)):
    AHEAD[_k].append(("K", 1, _n))
for _i in range(2 * PAIRS * NCH):
    AHEAD[4 + _i // 2].append(("MAX", _i))
for _j, _k in enumerate((12, 14, 16, 18, 20, 22, 24)):
    AHEAD[_k].append(("V", _j))
AHEAD[21].append(("SHIFT",))
ORDER = [item for at in AHEAD for item in at]
NV = -(-NT // 2)
NM = 2 * PAIRS * NCH
SPLIT_AT = (5, 9, 13, 17)
BANKS = 3
START_BANKS = BANKS + DC
OUT_ITEM = ("OUT",)
SHIFT_ITEM = ("SHIFT",)


def known(b, value):
    return isinstance(b, int) and b == value


def bank_numbers(b):
    if known(b, 0):
        return {item: i % START_BANKS for i, item in enumerate(i for i in ORDER if i != OUT_ITEM)}
    return {item: i % BANKS for i, item in enumerate(ORDER)}


def bank_before(b, item):
    mine = bank_numbers(b)
    seen = list(mine)[:list(mine).index(item)]
    same = [i for i in seen if mine[i] == mine[item] and not (i == OUT_ITEM and known(b, 1))]
    if same:
        return same[-1], b
    if known(b, 0):
        return None, None
    old = bank_numbers(b - 1)
    return [i for i in old if old[i] == mine[item]][-1], b - 1


def max_piece(i):
    return i // (PAIRS * NCH), i // NCH % PAIRS, i % NCH


def cols(n, real=False):
    return slice(n * CH, min((n + 1) * CH, T if real else TP))


def rows(t):
    return TLAST if t == NT - 1 else P


def cross_attention(nc, x1, ident, head_mask, x, ctx_t, wq, bq, wk, bk, wv, bv, wo, bo):
    with ExitStack() as ctx:
        def sb(name, shape, dt=F32):
            return ctx.enter_context(nc.sbuf_tensor(name, shape, dt))

        def ps(name, shape):
            return ctx.enter_context(nc.psum_tensor(name, shape, F32))

        def sem(name):
            return ctx.enter_context(nc.semaphore(name))

        raw = sb("raw", [P, NCH, DC, CH])
        ctx_hi = [sb(f"ctx_hi{i}", [P, DC, TP], F32R) for i in range(2)]
        ctx_lo = [sb(f"ctx_lo{i}", [P, DC, TP], F32R) for i in range(2)]
        k_hi = [sb(f"k_hi{i}", [P, DC, TP], F32R) for i in range(2)]
        k_lo = [sb(f"k_lo{i}", [P, DC, TP], F32R) for i in range(2)]
        v = [sb(f"v{i}", [P, NT, H, VW]) for i in range(2)]
        probs = [sb(f"probs{i}", [P, DC, COLS]) for i in range(2)]
        q_hi = sb("q_hi", [P, DC, B * NQ], F32R)
        q_lo = sb("q_lo", [P, DC, B * NQ], F32R)
        qb_hi = [sb(f"qb_hi{i}", [P, DC, HC, NQ], F32R) for i in range(2)]
        qb_lo = [sb(f"qb_lo{i}", [P, DC, HC, NQ], F32R) for i in range(2)]
        w_hi = sb("w_hi", [P, DC, 2 * D], F32R)
        w_lo = sb("w_lo", [P, DC, 2 * D], F32R)
        wo_pad = sb("wo_pad", [P, 4, D])
        shift = [sb(f"shift{i}", [P, 2 * PAIRS, P], F32R) for i in range(2)]
        ones = sb("ones", [P, P], F32R)
        bq_col = sb("bq_col", [P, DC])
        bk_col = sb("bk_col", [P, DC])
        bv_row = sb("bv_row", [P, D])
        bo_row = sb("bo_row", [P, D])
        maxima = sb("maxima", [P, 2 * PAIRS, NCH])
        neg_max = sb("neg_max", [P, 2 * PAIRS])
        o_sb = sb("o_sb", [P, 4 * NQ])
        o_sum = sb("o_sum", [P, 4 * NQ])
        o_rec = sb("o_rec", [P, 4 * NQ])
        o_n = sb("o_n", [P, 4, NQ])
        gate = sb("gate", [P, 1])
        stats = sb("stats", [P, TT, 6])
        mv = sb("mv", [P, TT, 2])
        rstd = sb("rstd", [P, TT])

        spare = v[1][:].rearrange("p t h w -> p (t h w)")
        x_in, xn = (spare[:, i * TT * D:(i + 1) * TT * D].rearrange("p (k d) -> p k d", k=TT) for i in range(2))
        xn_t = spare[:, 2 * TT * D:3 * TT * D].rearrange("p (c q) -> p c q", c=DC)
        q_f = xn_t
        w_raw = probs[0][:]
        wq_sb = probs[1][:, 0, :].rearrange("p (c n) -> p c n", c=DC)

        scores = [ps(f"scores{i}", [P, DC, COLS]) for i in range(2)]
        work = [ps(f"work{i}", [P, 512]) for i in range(BANKS)]
        o_ps = ps("o_ps", [P, 4 * NQ])

        raw_in = [sem(f"raw_in{n}") for n in range(NCH)]
        x_loaded = sem("x_loaded")
        w_loaded = sem("w_loaded")
        b_loaded = sem("b_loaded")
        wo_loaded = sem("wo_loaded")
        consts = sem("consts")
        wo_zeroed = sem("wo_zeroed")
        v_filled = sem("v_filled")
        pads = sem("pads")
        hi_done = sem("hi_done")
        lo_done = sem("lo_done")
        dve_step = sem("dve_step")
        std_done = sem("std_done")
        var_done = sem("var_done")
        xn_done = sem("xn_done")
        xt_full = sem("xt_full")
        xt_done = sem("xt_done")
        q_full = sem("q_full")
        q_split = sem("q_split")
        w_split = sem("w_split")
        qb_ready = sem("qb_ready")
        k_full = sem("k_full")
        khi_done = sem("khi_done")
        klo_done = sem("klo_done")
        v_full = sem("v_full")
        v_done = sem("v_done")
        m_full = sem("m_full")
        m_free = sem("m_free")
        negmax_ready = sem("negmax_ready")
        shift_full = sem("shift_full")
        shift_ready = sem("shift_ready")
        s_full = sem("s_full")
        exp_done = sem("exp_done")
        pv_done = sem("pv_done")
        o_copied = sem("o_copied")
        o_step = sem("o_step")
        o_ready = sem("o_ready")
        out_full = sem("out_full")
        out_added = sem("out_added")

        x_tok = x.rearrange("b q d -> (b q) d").rearrange("(k p) d -> p k d", p=P)

        def bank(b, item):
            return (work + [scores[0][:, c, :] for c in range(DC)])[bank_numbers(b)[item]]

        out_bank = work[bank_numbers(1)[OUT_ITEM]]
        block = ctx.enter_context(nc.Block())

        @block.sync
        def _(sp):
            sp.dma_start(x_in, x_tok).then_inc(x_loaded, 16)

            def load(b, n):
                c = cols(n, real=True)
                src = ctx_t[bass.ds(b, 1), :, c].rearrange("b (c p) t -> p (b c) t", p=P)
                sp.dma_start(raw[:, n, :, 0:c.stop - c.start], src).then_inc(raw_in[n], 16)

            sp.dma_start(w_raw[:, 0, :].rearrange("p (c n) -> p c n", c=DC),
                         wk.rearrange("(c p) n -> p c n", p=P)).then_inc(w_loaded, 16)
            load(0, 0)
            sp.dma_start(w_raw[:, 1, :].rearrange("p (c n) -> p c n", c=DC),
                         wv.rearrange("(c p) n -> p c n", p=P)).then_inc(w_loaded, 16)
            for n in range(1, NCH):
                load(0, n)
            with sp.Fori(1, B) as b:
                for n in range(NCH):
                    sp.wait_ge(lo_done, NCH * (b - 1) + n + 1)
                    load(b, n)

        @block.gpsimd
        def _(pool):
            pool.memset(ident[:], 0.0).then_inc(consts, 1)
            pool.memset(head_mask[:], 1.0).then_inc(consts, 1)
            pool.wait_ge(consts, 2)
            pool.affine_select(out=ident[:], in_=ident[:], compare_op=ALU.not_equal, fill=1.0, base=0,
                               pattern=[[-1, P]], channel_multiplier=1).then_inc(consts, 1)
            pool.affine_select(out=head_mask[:], in_=head_mask[:], compare_op=ALU.is_ge, fill=0.0, base=0,
                               pattern=[[-DH, HC]], channel_multiplier=1).then_inc(consts, 1)
            pool.wait_ge(consts, 4)
            pool.affine_select(out=head_mask[:], in_=head_mask[:], compare_op=ALU.is_ge, fill=0.0, base=DH - 1,
                               pattern=[[DH, HC]], channel_multiplier=-1).then_inc(consts, 1)
            pool.memset(wo_pad[:], 0.0).then_inc(wo_zeroed, 1)
            for i in range(2):
                pool.memset(ctx_hi[i][:, :, T:TP].bitcast(F32), 0.0).then_inc(pads, 1)
                pool.memset(ctx_lo[i][:, :, T:TP].bitcast(F32), 0.0).then_inc(pads, 1)
                pool.memset(shift[i][:].bitcast(F32), 0.0).then_inc(pads, 1)
            pool.memset(ones[:].bitcast(F32), 1.0).then_inc(pads, 1)
            pool.memset(v[0][:, :, :, DH:VW], 1.0).then_inc(v_filled, 1)

            def split_lo(b, par, n):
                c = cols(n, real=True)
                pool.wait_ge(hi_done, NCH * b + n + 1)
                pool.tensor_tensor(ctx_lo[par][:, :, c], raw[:, n, :, 0:c.stop - c.start],
                                   ctx_hi[par][:, :, c].bitcast(F32), ALU.subtract).then_inc(lo_done, 1)

            def spread_q(b, par):
                if not (known(b, 0) or known(b, 1)):
                    pool.wait_ge(s_full, NT * (b - 1))
                for c in range(DC):
                    for k, (src, dst) in enumerate(((q_hi, qb_hi[par]), (q_lo, qb_lo[par]))):
                        q = src[:, c, bass.ds(b * NQ, NQ)].bitcast(F32).unsqueeze(1).to_broadcast([P, HC, NQ])
                        m = head_mask[:].unsqueeze(2).to_broadcast([P, HC, NQ])
                        ins = pool.tensor_tensor(dst[:, c], q, m, ALU.mult)
                ins.then_inc(qb_ready, 1)

            for n in range(NCH):
                split_lo(0, 0, n)
            pool.wait_ge(q_split, 2 * DC)
            pool.wait_ge(consts, 5)
            spread_q(0, 0)
            pool.wait_ge(xn_done, 1)
            pool.memset(v[1][:, :, :, DH:VW], 1.0).then_inc(v_filled, 1)
            for n in range(NCH):
                split_lo(1, 1, n)

            def period(b, par, last=False, split=True):
                if not last:
                    spread_q(b + 1, 1 - par)
                if split:
                    for n in range(NCH):
                        split_lo(b + 2, par, n)

            period(0, 0)
            with pool.Fori(0, 2) as i:
                period(2 * i + 1, 1)
                period(2 * i + 2, 0)
            period(5, 1)
            period(6, 0, split=False)

        @block.tensor
        def _(pe):
            pe.wait_ge(consts, 3)
            pe.wait_ge(xn_done, 1)
            for c in range(DC):
                for k in range(TT):
                    ins = pe.transpose(scores[0][:, c, k * P:(k + 1) * P], xn[:, k, c * P:(c + 1) * P], ident[:])
            ins.then_inc(xt_full, 1)
            pe.wait_ge(xt_done, DC)
            pe.wait_ge(b_loaded, 16 * 5)
            for c in range(DC):
                for e in range(DC):
                    ins = pe.matmul(scores[1][:, c, :], wq_sb[:, e, c * P:(c + 1) * P], xn_t[:, e, :],
                                    start=(e == 0), stop=(e == DC - 1))
                ins.then_inc(q_full, 1)

            def bank_free(b, item):
                prev, nb = bank_before(b, item)
                if prev is None:
                    return
                if prev[0] == "K":
                    pe.wait_ge(klo_done, 2 * NCH * nb + prev[1] * NCH + prev[2] + 1)
                elif prev[0] == "V":
                    pe.wait_ge(v_done, NV * nb + prev[1] + 1)
                elif prev[0] == "SHIFT":
                    pe.wait_ge(shift_ready, nb + 1)
                elif prev[0] == "MAX":
                    pe.wait_ge(m_free, NM * nb + prev[1] + 1)
                elif prev[0] == "OUT":
                    pe.wait_ge(out_added, nb - 1)

            def project_k(b, par, c, n):
                pe.wait_ge(lo_done, NCH * b + n + 1)
                at = cols(n)
                terms = ((w_hi, ctx_hi), (w_lo, ctx_hi), (w_hi, ctx_lo))
                for j, (w, s) in enumerate(terms):
                    for e in range(DC):
                        ins = pe.matmul(bank(b, ("K", c, n))[:, 0:at.stop - at.start], w[:, e, c * P:(c + 1) * P], s[par][:, e, at],
                                        start=(j == 0 and e == 0), stop=(j == 2 and e == DC - 1))
                ins.then_inc(k_full, 1)

            def project_v(b, par, j):
                if j == 0:
                    pe.wait_ge(lo_done, NCH * (b + 1))
                terms = ((ctx_hi, w_hi), (ctx_hi, w_lo), (ctx_lo, w_hi))
                for t in range(2 * j, min(2 * j + 2, NT)):
                    r = rows(t)
                    o = bank(b, ("V", j))[0:r, (t % 2) * D:(t % 2 + 1) * D]
                    for e in range(DC):
                        for i, (s, w) in enumerate(terms):
                            ins = pe.matmul(o, s[par][:, e, t * P:t * P + r], w[:, e, D:2 * D],
                                            start=(e == 0 and i == 0), stop=(e == DC - 1 and i == 2))
                ins.then_inc(v_full, 1)

            def max_scores(b, par, i):
                c, p, n = max_piece(i)
                if i == 0:
                    pe.wait_ge(qb_ready, b + 1)
                if i % (PAIRS * NCH) < NCH:
                    pe.wait_ge(khi_done, 2 * NCH * b + NCH * c + n + 1)
                bank_free(b, ("MAX", i))
                at = cols(n)
                q = qb_hi[par][:, c].rearrange("p h q -> p (h q)")
                pe.matmul(bank(b, ("MAX", i))[:, 0:at.stop - at.start], q[:, p * P:(p + 1) * P], k_hi[par][:, c, at],
                          start=True, stop=True).then_inc(m_full, 1)

            def ahead(b, par, item):
                if item[0] == "K":
                    bank_free(b, item)
                    project_k(b, par, item[1], item[2])
                elif item[0] == "V":
                    bank_free(b, item)
                    project_v(b, par, item[1])
                elif item[0] == "MAX":
                    max_scores(b, par, item[1])
                elif item[0] == "SHIFT":
                    bank_free(b, item)
                    pe.wait_ge(negmax_ready, b + 1)
                    pe.transpose(bank(b, item)[0:2 * PAIRS, 0:P], neg_max[:], ident[:]).then_inc(shift_full, 1)

            def project_out(b, par):
                pe.wait_ge(o_ready, b + 1)
                for j in range(4):
                    ins = pe.matmul(out_bank[NQ * par:NQ * par + NQ, 0:D], o_n[:, j, :], wo_pad[:, j, :],
                                    start=(j == 0), stop=(j == 3))
                ins.then_inc(out_full, 1)

            def score(b, par, t):
                slot = (par * NT + t) % 2
                r = rows(t)
                if t == 0:
                    pe.wait_ge(shift_ready, b + 1)
                    if known(b, 0):
                        pe.wait_ge(v_done, NV)
                    pe.wait_ge(klo_done, 2 * NCH * (b + 1))
                if not (known(b, 0) and t < 2):
                    pe.wait_ge(exp_done, NT * b + t - 1)
                at = slice(t * P, t * P + r)
                for c in range(DC):
                    o = scores[slot][0:r, c, :]
                    qh, ql = (q[par][:, c].rearrange("p h q -> p (h q)") for q in (qb_hi, qb_lo))
                    sh = shift[par][:, c * PAIRS:(c + 1) * PAIRS, :].rearrange("p a n -> p (a n)")
                    pe.matmul(o, k_hi[par][:, c, at], qh, start=True, stop=False)
                    pe.matmul(o, k_hi[par][:, c, at], ql, start=False, stop=False)
                    pe.matmul(o, k_lo[par][:, c, at], qh, start=False, stop=False)
                    ins = pe.matmul(o, ones[:, 0:r], sh, start=False, stop=True)
                ins.then_inc(s_full, 1)

            def weigh(b, par, t):
                slot = (par * NT + t) % 2
                r = rows(t)
                if t % 2 == 0:
                    pe.wait_ge(v_done, NV * b + t // 2 + 1)
                if t == 0 and not known(b, 0):
                    pe.wait_ge(o_copied, b)
                pe.wait_ge(exp_done, NT * b + t + 1)
                for h in range(H):
                    g, j = h % 4, h // 4
                    c, hh = h // HC, h % HC
                    ins = pe.matmul(o_ps[32 * g:32 * g + VW, j * NQ:(j + 1) * NQ], v[par][0:r, t, h, :],
                                    probs[slot][0:r, c, hh * NQ:(hh + 1) * NQ], start=(t == 0 and j == 0),
                                    stop=(t == NT - 1), skip_group_check=True)
                ins.then_inc(pv_done, 1)

            def period(b, par, first=False, last=False):
                for t in range(NT):
                    if t < NT - 1:
                        score(b, par, t + 1)
                    elif not last:
                        score(b + 1, 1 - par, 0)
                    for k in (2 * t, 2 * t + 1):
                        if k % 2:
                            weigh(b, par, t)
                        for item in AHEAD[k]:
                            if item[0] == "OUT":
                                if not first:
                                    if last:
                                        pe.wait_ge(v_done, NV * (b + 1))
                                    else:
                                        bank_free(b + 1, item)
                                    project_out(b - 1, 1 - par)
                            elif not last:
                                ahead(b + 1, 1 - par, item)

            pe.wait_ge(w_split, 2)
            pe.wait_ge(pads, 7)
            for item in ORDER:
                if item[0] != "OUT":
                    ahead(0, 0, item)
            score(0, 0, 0)
            period(0, 0, first=True)
            pe.wait_ge(wo_loaded, 16 * 4)
            with pe.Fori(0, 2) as i:
                period(2 * i + 1, 1)
                period(2 * i + 2, 0)
            period(5, 1)
            period(6, 0)
            period(7, 1, last=True)
            pe.wait_ge(out_added, B - 1)
            project_out(B - 1, 1)

        @block.scalar
        def _(act):
            act.dma_start(wq_sb, wq.rearrange("(c p) n -> p c n", p=P)).then_inc(b_loaded, 16)
            act.dma_start(bq_col[:], bq).then_inc(b_loaded, 16)
            act.dma_start(bk_col[:], bk).then_inc(b_loaded, 16)
            act.dma_start(bv_row[:], bv.partition_broadcast(P)).then_inc(b_loaded, 16)
            act.dma_start(bo_row[:], bo.partition_broadcast(P)).then_inc(b_loaded, 16)
            act.wait_ge(wo_zeroed, 1)
            for g in range(4):
                act.dma_start(wo_pad[32 * g:32 * g + DH, :, :],
                              wo.rearrange("(j g r) n -> g r j n", g=4, r=DH)[g]).then_inc(wo_loaded, 16)
            act.wait_ge(var_done, 1)
            act.activation(rstd[:], mv[:, :, 1], ACT.Sqrt).then_inc(std_done, 1)
            act.wait_ge(b_loaded, 16 * 5)

            def keep_k_hi(b, par, c, n):
                at = cols(n)
                act.wait_ge(k_full, 2 * NCH * b + NCH * c + n + 1)
                act.activation(k_hi[par][:, c, at], bank(b, ("K", c, n))[:, 0:at.stop - at.start], ACT.Identity,
                               bias=bk_col[:, c:c + 1]).then_inc(khi_done, 1)

            def exponent(b, par, t):
                slot = (par * NT + t) % 2
                r = rows(t)
                act.wait_ge(s_full, NT * b + t + 1)
                if not (known(b, 0) and t < 2):
                    act.wait_ge(pv_done, NT * b + t - 1)
                act.activation(probs[slot][0:r], scores[slot][0:r], ACT.Exp).then_inc(exp_done, 1)

            def period(b, par, last=False):
                for t in range(NT):
                    if t < NT - 1:
                        exponent(b, par, t + 1)
                    elif not last:
                        exponent(b + 1, 1 - par, 0)
                    for k in (2 * t, 2 * t + 1):
                        for item in AHEAD[k]:
                            if item[0] == "K" and not last:
                                keep_k_hi(b + 1, 1 - par, item[1], item[2])

            for item in ORDER:
                if item[0] == "K":
                    keep_k_hi(0, 0, item[1], item[2])
            act.wait_ge(w_split, 2)
            act.wait_ge(q_full, DC)
            exponent(0, 0, 0)
            period(0, 0)
            with act.Fori(0, 2) as i:
                period(2 * i + 1, 1)
                period(2 * i + 2, 0)
            period(5, 1)
            period(6, 0)
            period(7, 1, last=True)

        @block.vector
        def _(dve):
            dve.wait_ge(x_loaded, 16)
            for k in range(TT):
                ins = dve.bn_stats(stats[:, k, :], x_in[:, k, :])
            ins.then_inc(dve_step, 1)
            dve.wait_ge(dve_step, 1)
            for k in range(TT):
                ins = dve.bn_aggr(mv[:, k, :], stats[:, k, :])
            ins.then_inc(dve_step, 1)
            dve.wait_ge(dve_step, 2)
            dve.tensor_scalar(mv[:, :, 1], mv[:, :, 1], LN_EPS, None, ALU.add).then_inc(var_done, 1)
            dve.wait_ge(w_loaded, 32)
            kv = "p k (c n) -> p c k n"
            w_src = w_raw.rearrange(kv, c=DC)
            dve.tensor_copy(w_hi[:].rearrange("p c (k n) -> p c k n", k=2), w_src).then_inc(w_split, 1)
            dve.wait_ge(std_done, 1)
            dve.reciprocal(rstd[:], rstd[:]).then_inc(dve_step, 1)
            dve.wait_ge(dve_step, 3)
            for k in range(TT):
                ins = dve.tensor_scalar(xn[:, k, :], x_in[:, k, :], mv[:, k, 0:1], rstd[:, k:k + 1],
                                        ALU.subtract, ALU.mult)
            ins.then_inc(xn_done, 1)

            def split_hi(b, par, n):
                c = cols(n, real=True)
                dve.wait_ge(raw_in[n], 16 * (b + 1))
                dve.tensor_copy(ctx_hi[par][:, :, c], raw[:, n, :, 0:c.stop - c.start]).then_inc(hi_done, 1)

            dve.wait_ge(w_split, 1)
            dve.tensor_tensor(w_lo[:].rearrange("p c (k n) -> p c k n", k=2), w_src,
                              w_hi[:].bitcast(F32).rearrange("p c (k n) -> p c k n", k=2),
                              ALU.subtract).then_inc(w_split, 1)
            split_hi(0, 0, 0)
            dve.wait_ge(xt_full, 1)
            for c in range(DC):
                dve.tensor_copy(xn_t[:, c, :], scores[0][:, c, :]).then_inc(xt_done, 1)
            for n in range(1, NCH):
                split_hi(0, 0, n)
            dve.wait_ge(b_loaded, 16 * 5)
            dve.tensor_tensor(x1[:], x_in, bo_row[:].unsqueeze(1).to_broadcast([P, TT, D]),
                              ALU.add).then_inc(dve_step, 1)
            dve.wait_ge(q_full, DC)
            for c in range(DC):
                dve.tensor_scalar(q_f[:, c, :], scores[1][:, c, :], bq_col[:, c:c + 1], DH ** -0.5,
                                  ALU.add, ALU.mult).then_inc(dve_step, 1)
                dve.wait_ge(dve_step, 5 + c)
                dve.tensor_copy(q_hi[:, c, :], q_f[:, c, :]).then_inc(q_split, 1)
                dve.wait_ge(q_split, 2 * c + 1)
                dve.tensor_tensor(q_lo[:, c, :], q_f[:, c, :], q_hi[:, c, :].bitcast(F32),
                                  ALU.subtract).then_inc(q_split, 1)

            def keep_k_lo(b, par, c, n):
                at = cols(n)
                dve.wait_ge(khi_done, 2 * NCH * b + NCH * c + n + 1)
                src = bank(b, ("K", c, n))[:, 0:at.stop - at.start]
                dve.scalar_tensor_tensor(k_lo[par][:, c, at], src, bk_col[:, c:c + 1],
                                         k_hi[par][:, c, at].bitcast(F32), ALU.add,
                                         ALU.subtract).then_inc(klo_done, 1)

            def keep_v(b, par, j):
                dve.wait_ge(v_full, NV * b + j + 1)
                nt = min(2, NT - 2 * j)
                r = rows(2 * j)
                dve.tensor_tensor(
                    v[par][0:r, 2 * j:2 * j + nt, :, 0:DH],
                    bank(b, ("V", j))[0:r, 0:nt * D].rearrange("p (t h d) -> p t h d", t=nt, h=H),
                    bv_row[0:r].rearrange("p (h d) -> p h d", h=H).unsqueeze(1).to_broadcast([r, nt, H, DH]),
                    ALU.add).then_inc(v_done, 1)

            def keep_max(b, i):
                c, p, n = max_piece(i)
                at = cols(n, real=True)
                dve.wait_ge(m_full, NM * b + i + 1)
                dve.tensor_reduce(maxima[:, c * PAIRS + p, n:n + 1], bank(b, ("MAX", i))[:, 0:at.stop - at.start], AX.X,
                                  ALU.max).then_inc(m_free, 1)
                if i == NM - 1:
                    dve.wait_ge(m_free, NM * (b + 1))
                    dve.tensor_reduce(neg_max[:], maxima[:], AX.X, ALU.max,
                                      negate=True).then_inc(negmax_ready, 1)

            def keep_shift(b, par):
                dve.wait_ge(shift_full, b + 1)
                n = 2 * PAIRS
                dve.tensor_tensor(shift[par][0:n], bank(b, SHIFT_ITEM)[0:n, 0:P].unsqueeze(1).to_broadcast([n, n, P]),
                                  ident[0:n, 0:n].unsqueeze(2).to_broadcast([n, n, P]),
                                  ALU.mult).then_inc(shift_ready, 1)

            def ahead(b, par, item):
                if item[0] == "K":
                    keep_k_lo(b, par, item[1], item[2])
                elif item[0] == "V":
                    keep_v(b, par, item[1])
                elif item[0] == "MAX":
                    keep_max(b, item[1])
                elif item[0] == "SHIFT":
                    keep_shift(b, par)

            def finish_sums(b):
                dve.wait_ge(pv_done, NT * (b + 1))
                dve.tensor_copy(o_sb[:], o_ps[:]).then_inc(o_copied, 1)
                dve.wait_ge(o_copied, b + 1)
                dve.memset(gate[:], 0.0)
                dve.stream_shuffle(o_sum[:], o_sb[:], [DH] * 32).then_inc(o_step, 1)
                dve.wait_ge(o_step, 2 * b + 1)
                dve.reciprocal(o_rec[:], o_sum[:]).then_inc(o_step, 1)
                dve.wait_ge(o_step, 2 * b + 2)
                dve.tensor_tensor(o_n[:].rearrange("p j q -> p (j q)"), o_sb[:], o_rec[:],
                                  ALU.mult).then_inc(o_ready, 1)

            def add_out(b, par, pair):
                dve.wait_ge(out_full, b + 1)
                at = slice(NQ * par, NQ * par + NQ)
                dst = x1[at, bass.ds(pair, 1), :].rearrange("p k d -> p (k d)")
                dve.tensor_tensor(dst, out_bank[at, 0:D], dst, ALU.add).then_inc(out_added, 1)

            def period(b, par, pair, first=False, last=False, split=True):
                if not first:
                    finish_sums(b - 1)
                for k in range(POS):
                    for item in AHEAD[k]:
                        if item[0] == "OUT":
                            if not first:
                                add_out(b - 1, 1 - par, pair)
                        elif not last:
                            ahead(b + 1, 1 - par, item)
                    if split and k in SPLIT_AT:
                        split_hi(b + 2, par, SPLIT_AT.index(k))

            dve.memset(o_ps[:], 0.0).then_inc(dve_step, 1)
            for item in ORDER:
                if item[0] != "OUT":
                    ahead(0, 0, item)
            for n in range(NCH):
                split_hi(1, 1, n)
            period(0, 0, None, first=True)
            with dve.Fori(0, 2) as i:
                period(2 * i + 1, 1, i)
                period(2 * i + 2, 0, i)
            period(5, 1, 2)
            period(6, 0, 2, split=False)
            period(7, 1, 3, last=True, split=False)
            finish_sums(B - 1)
            add_out(B - 1, 1, 3)


def rope_table(base):
    freq = np.float32(1.0) / np.float32(base) ** (np.arange(0, DH, 2, dtype=np.float32) / np.float32(DH))
    angle = np.arange(NQ, dtype=np.float32)[:, None] * freq[None, :].astype(np.float32)
    cos, sin = np.cos(angle), np.sin(angle)
    return np.stack([np.stack([cos, cos], -1), np.stack([-sin, sin], -1)], 1).reshape(NQ, 2, DH)


def shape_constants():
    tables = np.stack([rope_table(1e6), rope_table(1e4)], 1).reshape(NQ, 4 * DH)
    causal = np.arange(NQ)[None, :] >= np.arange(NQ)[:, None]
    rank = np.broadcast_to(np.arange(E, 0, -1), (NQ, E))
    one = np.concatenate([tables, causal, rank], 1).astype(np.float32)
    return np.concatenate([one, one], 0)


def latent_layers(nc, x1, ident, head_mask, consts, norm_w, g_wq, g_down, g_up, g_wo, l_wqkv, l_wo,
                  router_w, router_b, expert_w, expert_b, out):
    with ExitStack() as ctx:
        def sb(name, shape, dt=F32):
            return ctx.enter_context(nc.sbuf_tensor(name, shape, dt))

        def ps(name, shape):
            return ctx.enter_context(nc.psum_tensor(name, shape, F32))

        sems = {}

        def S(name):
            if name not in sems:
                sems[name] = ctx.enter_context(nc.semaphore("t_" + name))
            return sems[name]

        QK = (H + KV) * DH
        QKV = (H + 2 * KV) * DH
        REP = H // KV
        const = sb("const", [P, 4 * DH + NQ + E])
        table = [[const[:, (2 * i + j) * DH:(2 * i + j + 1) * DH] for j in range(2)] for i in range(2)]
        causal = const[:, 4 * DH:4 * DH + NQ]
        rank = const[:, 4 * DH + NQ:]
        norm_row = sb("norm_row", [P, 2, D])
        gq = sb("gq", [P, DC, D])
        gdown = sb("gdown", [P, DC, LAT])
        gup = sb("gup", [LAT, 2 * KV * DH])
        lqkv = sb("lqkv", [P, DC, QKV])
        w_out = [sb(f"w_out{i}", [P, DC, D]) for i in range(2)]
        rw = sb("rw", [P, DC, E])
        rb = sb("rb", [P, E])
        ew = sb("ew", [P, DC, E * D])
        eb = sb("eb", [E, D])

        a = sb("a", [P, TT, D])
        hn = sb("hn", [P, TT, D])
        h_t = sb("h_t", [P, DC, TT * P])
        lat_t = sb("lat_t", [LAT, TT * P])
        squares = sb("squares", [P, TT, QK])
        ms = sb("ms", [P, TT])
        rms = sb("rms", [P, TT])
        ms2 = sb("ms2", [P, TT, H + KV])
        rq = sb("rq", [P, TT, H + KV])
        t1 = sb("t1", [P, TT, QK])
        t2 = sb("t2", [P, TT, QK])
        roped = sb("roped", [P, TT, QK])
        qn = sb("qn", [P, TT, D])
        kn = sb("kn", [P, TT, D])
        vt = sb("vt", [P, TT, KV, VW])
        k_t = sb("k_t", [P, TT, DC, P])
        q_bd = sb("q_bd", [P, TT, DC, HC, P])
        e_s = sb("e_s", [P, TT, DC, HC, NQ])
        p_t = sb("p_t", [P, TT, DC, HC, NQ])
        rec = sb("rec", [P, TT, H])
        on = sb("on", [P, TT, D])
        o_t = sb("o_t", [P, TT, DC, P])
        stats = sb("t_stats", [P, TT, 6])
        mv = sb("t_mv", [P, TT, 2])
        rstd = sb("t_rstd", [P, TT])
        lg = sb("lg", [P, TT, E])
        ex = sb("ex", [P, TT, E])
        pr = sb("pr", [P, TT, E])
        hit = sb("hit", [P, TT, E])
        wgt = sb("wgt", [P, TT, E])
        lmax = sb("lmax", [P, TT])
        lsum = sb("lsum", [P, TT])
        lrec = sb("lrec", [P, TT])
        pmax = sb("pmax", [P, TT])
        first = sb("first", [P, TT])
        wgt_t = sb("wgt_t", [E, TT, P])

        tp = [ps(f"tp{i}", [P, 4, P]) for i in range(2)]
        qk = [ps(f"qk{i}", [P, 512]) for i in range(2)]
        sc = [ps(f"sc{i}", [P, 512]) for i in range(2)]
        ob = [ps(f"ob{i}", [P, 512]) for i in range(2)]

        out_tok = out.rearrange("b q d -> (b q) d").rearrange("(k p) d -> p k d", p=P)
        block = ctx.enter_context(nc.Block())

        @block.sync
        def _(sp):
            rows_of = "(c p) n -> p c n"
            sp.dma_start(norm_row[:].rearrange("p c n -> p (c n)"), norm_w.partition_broadcast(P)).then_inc(S("norm_in"), 16)
            sp.dma_start(gq[:], g_wq.rearrange(rows_of, p=P)).then_inc(S("gq_in"), 16)
            sp.dma_start(gdown[:], g_down.rearrange(rows_of, p=P)).then_inc(S("gkv_in"), 16)
            sp.dma_start(gup[:], g_up).then_inc(S("gkv_in"), 16)
            sp.dma_start(const[:], consts).then_inc(S("const_in"), 16)
            sp.dma_start(w_out[0][:], g_wo.rearrange(rows_of, p=P)).then_inc(S("wo_in"), 16)
            sp.dma_start(lqkv[:], l_wqkv.rearrange(rows_of, p=P)).then_inc(S("lqkv_in"), 16)
            sp.dma_start(w_out[1][:], l_wo.rearrange(rows_of, p=P)).then_inc(S("wo_in"), 16)
            sp.dma_start(rw[:], router_w.rearrange(rows_of, p=P)).then_inc(S("router_in"), 16)
            sp.dma_start(rb[:], router_b.partition_broadcast(P)).then_inc(S("router_in"), 16)
            sp.dma_start(eb[:], expert_b).then_inc(S("router_in"), 16)
            sp.dma_start(ew[:], expert_w.rearrange(rows_of, p=P)).then_inc(S("experts_in"), 16)
            for k in range(TT):
                sp.wait_ge(S("mixed"), E * (k + 1))
                sp.dma_start(out_tok[:, k, :], x1[:, k, :]).then_inc(S("stored"), 16)
            sp.wait_ge(S("stored"), 16 * TT)

        @block.gpsimd
        def _(pool):
            pool.memset(vt[:, :, :, DH:VW], 1.0).then_inc(S("v_ones"), 1)
            pool.wait_ge(S("const_in"), 16)
            for L in range(2):
                for k in range(TT):
                    pool.wait_ge(S("t2"), TT * L + k + 1)
                    pool.tensor_tensor(roped[:, k, :], t1[:, k, :], t2[:, k, :], ALU.add).then_inc(S("roped"), 1)
                for k in range(TT):
                    for c in range(DC):
                        n = DC * (TT * L + k) + c + 1
                        pool.wait_ge(S("exp"), n)
                        pool.tensor_tensor(p_t[:, k, c], e_s[:, k, c],
                                           causal.unsqueeze(1).to_broadcast([P, HC, NQ]),
                                           ALU.mult).then_inc(S("masked"), 1)

        @block.tensor
        def _(pe):
            def turn(src, k, name, ready):
                pe.wait_ge(S(ready[0]), ready[1])
                for c in range(DC):
                    ins = pe.transpose(tp[k % 2][:, c, :], src[:, k, c * P:(c + 1) * P], ident[:])
                ins.then_inc(S(name), 1)

            for L in range(2):
                n0 = TT * L
                for k in range(TT):
                    n = n0 + k + 1
                    if k >= 2:
                        pe.wait_ge(S("h_t"), n - 2)
                    elif L:
                        pe.wait_ge(S("o_t"), n0)
                    turn(hn, k, "h_turned", ("hn", n))
                if L == 0:
                    pe.wait_ge(S("gkv_in"), 32)
                    pe.wait_ge(S("gq_in"), 16)
                    for k in range(TT):
                        pe.wait_ge(S("h_t"), k + 1)
                        if k >= 2:
                            pe.wait_ge(S("lat_t"), k - 1)
                        for c in range(DC):
                            ins = pe.matmul(ob[k % 2][0:LAT, 0:P], gdown[:, c, :], h_t[:, c, k * P:(k + 1) * P],
                                            start=(c == 0), stop=(c == DC - 1))
                        ins.then_inc(S("lat"), 1)
                else:
                    pe.wait_ge(S("lqkv_in"), 16)
                for k in range(TT):
                    n = n0 + k + 1
                    pe.wait_ge(S("h_t"), n)
                    if n > 2:
                        pe.wait_ge(S("t2"), n - 2)
                        pe.wait_ge(S("v"), n - 2)
                    o = qk[k % 2]
                    for c in range(DC):
                        h = h_t[:, c, k * P:(k + 1) * P]
                        if L == 0:
                            pe.matmul(o[:, 0:D], h, gq[:, c, :], start=(c == 0), stop=(c == DC - 1))
                        else:
                            ins = pe.matmul(o[:, 0:QKV], h, lqkv[:, c, :], start=(c == 0), stop=(c == DC - 1))
                    if L == 0:
                        pe.wait_ge(S("lat_t"), k + 1)
                        ins = pe.matmul(o[:, D:QKV], lat_t[:, k * P:(k + 1) * P], gup[:], start=True, stop=True)
                    ins.then_inc(S("qkv"), 1)
                for k in range(TT):
                    n = n0 + k + 1
                    pe.wait_ge(S("kn"), n)
                    if k < 2:
                        pe.wait_ge(S("h_t"), n0 + TT)
                    else:
                        pe.wait_ge(S("q_bd"), n - 2)
                        pe.wait_ge(S("k_t"), n - 2)
                    for i, src in enumerate((qn, kn)):
                        for c in range(DC):
                            ins = pe.transpose(tp[k % 2][:, 2 * i + c, :], src[:, k, c * P:(c + 1) * P], ident[:])
                    ins.then_inc(S("qk_turned"), 1)
                for k in range(TT):
                    n = n0 + k + 1
                    pe.wait_ge(S("k_t"), n)
                    pe.wait_ge(S("q_bd"), n)
                    for c in range(DC):
                        if n > 1:
                            pe.wait_ge(S("exp"), DC * (n - 1) + c - 1)
                        for s in range(2):
                            at = slice(s * NQ, (s + 1) * NQ)
                            ins = pe.matmul(sc[c][at, :], k_t[:, k, c, at], q_bd[:, k, c, :, at], start=True, stop=True)
                        ins.then_inc(S("scores"), 1)
                for k in range(TT):
                    n = n0 + k + 1
                    pe.wait_ge(S("masked"), DC * n)
                    if k >= 2:
                        pe.wait_ge(S("on"), n - 2)
                    elif L == 0:
                        pe.wait_ge(S("lat_t"), TT)
                        pe.wait_ge(S("v_ones"), 1)
                    else:
                        pe.wait_ge(S("a"), TT)
                    for h in range(H):
                        for s in range(2):
                            at = slice(s * NQ, (s + 1) * NQ)
                            ins = pe.matmul(ob[k % 2][at, h * VW:(h + 1) * VW], p_t[at, k, h // HC, h % HC, :],
                                            vt[at, k, h // REP, :], start=True, stop=True)
                    ins.then_inc(S("weighed"), 1)
                for k in range(TT):
                    n = n0 + k + 1
                    if k >= 2:
                        pe.wait_ge(S("o_t"), n - 2)
                    else:
                        pe.wait_ge(S("q_bd"), n0 + TT)
                        pe.wait_ge(S("k_t"), n0 + TT)
                    turn(on, k, "o_turned", ("on", n))
                pe.wait_ge(S("wo_in"), 32)
                for k in range(TT):
                    n = n0 + k + 1
                    pe.wait_ge(S("o_t"), n)
                    if k >= 2:
                        pe.wait_ge(S("a"), n - 2)
                    else:
                        pe.wait_ge(S("on"), n0 + TT)
                    for c in range(DC):
                        ins = pe.matmul(ob[k % 2][:, 0:D], o_t[:, k, c, :], w_out[L][:, c, :],
                                        start=(c == 0), stop=(c == DC - 1))
                    ins.then_inc(S("projected"), 1)

            pe.wait_ge(S("router_in"), 48)
            for k in range(TT):
                if k < 2:
                    pe.wait_ge(S("o_t"), 2 * TT)
                else:
                    pe.wait_ge(S("m_t"), k - 1)
                turn(hn, k, "m_turned", ("mn", k + 1))
            for k in range(TT):
                pe.wait_ge(S("m_t"), k + 1)
                if k == 0:
                    pe.wait_ge(S("a"), 2 * TT)
                for c in range(DC):
                    ins = pe.matmul(ob[0][:, k * E:(k + 1) * E], h_t[:, c, k * P:(k + 1) * P], rw[:, c, :],
                                    start=(c == 0), stop=(c == DC - 1))
            ins.then_inc(S("logits"), 1)

            banks = [qk[0], qk[1], sc[0], sc[1]]

            def experts(k, i):
                u = k * (E // 2) + i
                if u < 2:
                    pe.wait_ge(S("t2"), 2 * TT)
                    pe.wait_ge(S("v"), 2 * TT)
                elif u < 4:
                    pe.wait_ge(S("exp"), 2 * TT * DC)
                else:
                    pe.wait_ge(S("mixed"), 2 * (u - 3))
                for c in range(DC):
                    ins = pe.matmul(banks[u % 4][:], h_t[:, c, k * P:(k + 1) * P], ew[:, c, i * 2 * D:(i + 1) * 2 * D],
                                    start=(c == 0), stop=(c == DC - 1))
                ins.then_inc(S("expert"), 1)

            pe.wait_ge(S("experts_in"), 16)
            for i in range(E // 2):
                experts(0, i)
            pe.wait_ge(S("wgt"), 1)
            for k in range(TT):
                ins = pe.transpose(tp[0][0:E, k, :], wgt[:, k, :], ident[:])
            ins.then_inc(S("w_turned"), 1)
            pe.wait_ge(S("w_t"), 1)
            for k in range(TT):
                pe.matmul(ob[k // 2][:, (k % 2) * D:(k % 2 + 1) * D], wgt_t[:, k, :], eb[:], start=True,
                          stop=True).then_inc(S("bias"), 1)
            for k in range(1, TT):
                for i in range(E // 2):
                    experts(k, i)

        @block.scalar
        def _(act):
            act.wait_ge(S("var"), 1)
            act.activation(rstd[:], mv[:, :, 1], ACT.Sqrt).then_inc(S("std"), 1)
            for L in range(2):
                n0 = TT * L
                for k in range(TT):
                    n = n0 + k + 1
                    act.wait_ge(S("a_in") if L == 0 else S("a"), k + 1)
                    if n > 1:
                        act.wait_ge(S("squared"), n - 1)
                    act.activation(squares[:, 0, 0:D], a[:, k, :], ACT.Square, scale=D ** -0.5,
                                   accum_out=ms[:, k:k + 1]).then_inc(S("squared"), 1)
                act.wait_ge(S("ms"), L + 1)
                act.activation(rms[:], ms[:], ACT.Sqrt).then_inc(S("rms"), 1)
                for k in range(TT):
                    act.wait_ge(S("h_turned"), n0 + k + 1)
                    act.activation(h_t[:, :, k * P:(k + 1) * P], tp[k % 2][:, 0:DC, :], ACT.Copy).then_inc(S("h_t"), 1)
                if L == 0:
                    for k in range(TT):
                        act.wait_ge(S("lat"), k + 1)
                        act.activation(lat_t[:, k * P:(k + 1) * P], ob[k % 2][0:LAT, 0:P],
                                       ACT.Copy).then_inc(S("lat_t"), 1)
                for k in range(TT):
                    n = n0 + k + 1
                    act.wait_ge(S("qkv"), n)
                    if k == 0:
                        act.wait_ge(S("squared"), n0 + TT)
                    act.activation(squares[:, k, :], qk[k % 2][:, 0:QK], ACT.Square,
                                   scale=DH ** -0.5).then_inc(S("sq2"), 1)
                    if L and k == 0:
                        act.wait_ge(S("weighed"), TT)
                    if n == 1:
                        act.wait_ge(S("v_ones"), 1)
                    act.activation(vt[:, k, :, 0:DH], qk[k % 2][:, QK:QKV].rearrange("p (g d) -> p g d", g=KV),
                                   ACT.Copy).then_inc(S("v"), 1)
                for k in range(TT):
                    act.wait_ge(S("ms2"), n0 + k + 1)
                    act.activation(rq[:, k, :], ms2[:, k, :], ACT.Sqrt).then_inc(S("rms2"), 1)
                for k in range(TT):
                    act.wait_ge(S("qk_turned"), n0 + k + 1)
                    act.activation(k_t[:, k], tp[k % 2][:, DC:2 * DC, :], ACT.Copy).then_inc(S("k_t"), 1)
                for k in range(TT):
                    for c in range(DC):
                        n = DC * (n0 + k) + c + 1
                        act.wait_ge(S("scores"), n)
                        if L:
                            act.wait_ge(S("masked"), n - DC * TT)
                        act.activation(e_s[:, k, c].rearrange("p h q -> p (h q)"), sc[c][:], ACT.Exp,
                                       scale=DH ** -0.5).then_inc(S("exp"), 1)
                for k in range(TT):
                    act.wait_ge(S("o_turned"), n0 + k + 1)
                    act.activation(o_t[:, k], tp[k % 2][:, 0:DC, :], ACT.Copy).then_inc(S("o_t"), 1)
            act.wait_ge(S("var"), 2)
            act.activation(rstd[:], mv[:, :, 1], ACT.Sqrt).then_inc(S("std"), 1)
            for k in range(TT):
                act.wait_ge(S("m_turned"), k + 1)
                act.activation(h_t[:, :, k * P:(k + 1) * P], tp[k % 2][:, 0:DC, :], ACT.Copy).then_inc(S("m_t"), 1)
            act.wait_ge(S("lg_shifted"), 1)
            act.activation(ex[:], lg[:], ACT.Exp).then_inc(S("lg_exp"), 1)

        @block.vector
        def _(dve):
            steps = [0]

            def link(ins):
                steps[0] += 1
                ins.then_inc(S("dve_step"), 1)
                dve.wait_ge(S("dve_step"), steps[0])

            def layer_norm(dst, name, turn):
                for k in range(TT):
                    ins = dve.bn_stats(stats[:, k, :], x1[:, k, :])
                link(ins)
                for k in range(TT):
                    ins = dve.bn_aggr(mv[:, k, :], stats[:, k, :])
                link(ins)
                dve.tensor_scalar(mv[:, :, 1], mv[:, :, 1], LN_EPS, None, ALU.add).then_inc(S("var"), 1)
                dve.wait_ge(S("std"), turn)
                link(dve.reciprocal(rstd[:], rstd[:]))
                for k in range(TT):
                    dve.tensor_scalar(dst[:, k, :], x1[:, k, :], mv[:, k, 0:1], rstd[:, k:k + 1],
                                      ALU.subtract, ALU.mult).then_inc(S(name), 1)

            layer_norm(a, "a_in", 1)
            for L in range(2):
                n0 = TT * L
                dve.wait_ge(S("squared"), n0 + TT)
                dve.tensor_scalar(ms[:], ms[:], RMS_EPS, None, ALU.add).then_inc(S("ms"), 1)
                dve.wait_ge(S("rms"), L + 1)
                link(dve.reciprocal(rms[:], rms[:]))
                if L == 0:
                    dve.wait_ge(S("norm_in"), 16)
                    dve.wait_ge(S("a_in"), TT)
                for k in range(TT):
                    dve.scalar_tensor_tensor(hn[:, k, :], a[:, k, :], rms[:, k:k + 1], norm_row[:, L, :],
                                             ALU.mult, ALU.mult).then_inc(S("hn"), 1)
                if L == 0:
                    dve.wait_ge(S("const_in"), 16)

                def rotate(k):
                    n = n0 + k + 1
                    dve.wait_ge(S("v"), n)
                    if L:
                        dve.wait_ge(S("roped"), TT)
                    x = qk[k % 2][:, 0:QK].rearrange("p (h d) -> p h d", d=DH)
                    cos = table[L][0].unsqueeze(1).to_broadcast([P, H + KV, DH])
                    dve.tensor_tensor(t1[:, k, :].rearrange("p (h d) -> p h d", d=DH), x, cos,
                                      ALU.mult).then_inc(S("t1"), 1)
                    sin = table[L][1].unsqueeze(1).to_broadcast([P, H + KV, DH])
                    y = t2[:, k, :].rearrange("p (h d) -> p h d", d=DH)
                    dve.tensor_tensor(y[:, :, 0::2], x[:, :, 1::2], sin[:, :, 0::2], ALU.mult).then_inc(S("t1"), 1)
                    dve.wait_ge(S("t1"), 2 * n)
                    dve.tensor_tensor(y[:, :, 1::2], x[:, :, 0::2], sin[:, :, 1::2], ALU.mult).then_inc(S("t2"), 1)
                    dve.wait_ge(S("sq2"), n)
                    link(dve.tensor_reduce(ms2[:, k, :], squares[:, k, :].rearrange("p (h d) -> p h d", d=DH),
                                           AX.X, ALU.add))
                    dve.tensor_scalar(ms2[:, k, :], ms2[:, k, :], RMS_EPS, None, ALU.add).then_inc(S("ms2"), 1)

                def normalise(k):
                    n = n0 + k + 1
                    dve.wait_ge(S("rms2"), n)
                    link(dve.reciprocal(rq[:, k, :], rq[:, k, :]))
                    dve.wait_ge(S("roped"), n)
                    x = roped[:, k, :].rearrange("p (h d) -> p h d", d=DH)
                    dve.tensor_tensor(qn[:, k, :].rearrange("p (h d) -> p h d", d=DH), x[:, 0:H],
                                      rq[:, k, 0:H].unsqueeze(2).to_broadcast([P, H, DH]), ALU.mult)
                    dve.tensor_tensor(
                        kn[:, k, :].rearrange("p (g r d) -> p g r d", g=KV, r=REP),
                        x[:, H:].unsqueeze(2).to_broadcast([P, KV, REP, DH]),
                        rq[:, k, H:].unsqueeze(2).unsqueeze(3).to_broadcast([P, KV, REP, DH]),
                        ALU.mult).then_inc(S("kn"), 1)

                for k in range(TT):
                    rotate(k)
                for k in range(TT):
                    normalise(k)
                for k in range(TT):
                    n = n0 + k + 1
                    dve.wait_ge(S("k_t"), n)
                    for c in range(DC):
                        ins = dve.tensor_tensor(q_bd[:, k, c], tp[k % 2][:, c, :].unsqueeze(1).to_broadcast([P, HC, P]),
                                                head_mask[:].unsqueeze(2).to_broadcast([P, HC, P]), ALU.mult)
                    ins.then_inc(S("q_bd"), 1)
                for k in range(TT):
                    n = n0 + k + 1
                    dve.wait_ge(S("weighed"), n)
                    o = ob[k % 2][:, 0:H * VW].rearrange("p (h w) -> p h w", w=VW)
                    link(dve.reciprocal(rec[:, k, :], o[:, :, DH]))
                    dve.tensor_tensor(on[:, k, :].rearrange("p (h d) -> p h d", d=DH), o[:, :, 0:DH],
                                      rec[:, k, :].unsqueeze(2).to_broadcast([P, H, DH]), ALU.mult).then_inc(S("on"), 1)
                for k in range(TT):
                    n = n0 + k + 1
                    dve.wait_ge(S("projected"), n)
                    dve.tensor_tensor(a[:, k, :], ob[k % 2][:, 0:D], a[:, k, :], ALU.add).then_inc(S("a"), 1)
            dve.wait_ge(S("a"), 2 * TT)
            link(dve.tensor_tensor(x1[:], x1[:], a[:], ALU.add))
            layer_norm(hn, "mn", 2)

            def over(t):
                return t[:].unsqueeze(2).to_broadcast([P, TT, E])

            dve.wait_ge(S("logits"), 1)
            link(dve.tensor_tensor(lg[:], ob[0][:, 0:TT * E].rearrange("p (k e) -> p k e", e=E),
                                   rb[:].unsqueeze(1).to_broadcast([P, TT, E]), ALU.add))
            link(dve.tensor_reduce(lmax[:], lg[:], AX.X, ALU.max))
            dve.tensor_tensor(lg[:], lg[:], over(lmax), ALU.subtract).then_inc(S("lg_shifted"), 1)
            dve.wait_ge(S("lg_exp"), 1)
            link(dve.tensor_reduce(lsum[:], ex[:], AX.X, ALU.add))
            link(dve.reciprocal(lrec[:], lsum[:]))
            link(dve.tensor_tensor(pr[:], ex[:], over(lrec), ALU.mult))
            link(dve.tensor_reduce(pmax[:], pr[:], AX.X, ALU.max))
            link(dve.tensor_tensor(hit[:], pr[:], over(pmax), ALU.is_equal))
            link(dve.tensor_tensor(hit[:], hit[:], rank.unsqueeze(1).to_broadcast([P, TT, E]), ALU.mult))
            link(dve.tensor_reduce(first[:], hit[:], AX.X, ALU.max))
            link(dve.tensor_tensor(hit[:], hit[:], over(first), ALU.is_equal))
            dve.tensor_tensor(wgt[:], hit[:], over(pmax), ALU.mult).then_inc(S("wgt"), 1)
            dve.wait_ge(S("w_turned"), 1)
            dve.tensor_copy(wgt_t[:], tp[0][0:E]).then_inc(S("w_t"), 1)
            for j in range(TT // 2):
                dve.wait_ge(S("bias"), 2 * j + 2)
                at = x1[:, 2 * j:2 * j + 2, :]
                link(dve.tensor_tensor(at, ob[j][:].rearrange("p (k d) -> p k d", d=D), at, ALU.add))
            banks = [qk[0], qk[1], sc[0], sc[1]]
            for k in range(TT):
                for e in range(E):
                    u = k * (E // 2) + e // 2
                    dve.wait_ge(S("expert"), u + 1)
                    if e:
                        dve.wait_ge(S("mixed"), E * k + e)
                    dve.scalar_tensor_tensor(x1[:, k, :], banks[u % 4][:, (e % 2) * D:(e % 2 + 1) * D],
                                             wgt[:, k, e:e + 1], x1[:, k, :], ALU.mult,
                                             ALU.add).then_inc(S("mixed"), 1)


def perceiver_kernel(nc, cross, latent, out):
    with ExitStack() as ctx:
        x1 = ctx.enter_context(nc.sbuf_tensor("x1", [P, TT, D], F32))
        ident = ctx.enter_context(nc.sbuf_tensor("ident", [P, P], F32))
        head_mask = ctx.enter_context(nc.sbuf_tensor("head_mask", [P, HC], F32))
        cross_attention(nc, x1, ident, head_mask, **cross)
        latent_layers(nc, x1, ident, head_mask, out=out, **latent)


def kernel(**inputs):
    from concourse import bacc
    from concourse.bass_utils import run_bass_kernel_spmd

    def of(name):
        return np.asarray(inputs[name])

    nc = bacc.Bacc("TRN2", target_bir_lowering=False, num_devices=1)
    cross = {
        "x": of("x"),
        "ctx_t": np.transpose(of("ctx_1024"), (0, 2, 1)),
        "wq": of("L0_xattn_Wq"), "bq": np.reshape(of("L0_xattn_bq"), (DC, P)).T,
        "wk": of("L0_xattn_Wk"), "bk": np.reshape(of("L0_xattn_bk"), (DC, P)).T,
        "wv": of("L0_xattn_Wv"), "bv": of("L0_xattn_bv"),
        "wo": of("L0_xattn_Wo"), "bo": of("L0_xattn_bo"),
    }
    latent = {
        "consts": shape_constants(),
        "norm_w": np.concatenate([of("L0_attn_norm1_w"), of("L0_attn_norm2_w")]),
        "g_wq": of("L0_attn_g_wq"), "g_down": of("L0_attn_g_kv_down"),
        "g_up": np.concatenate([of("L0_attn_g_k_up"), of("L0_attn_g_v_up")], 1),
        "g_wo": of("L0_attn_g_wo"),
        "l_wqkv": np.concatenate([of("L0_attn_l_wq"), of("L0_attn_l_wk"), of("L0_attn_l_wv")], 1),
        "l_wo": of("L0_attn_l_wo"),
        "router_w": of("L0_ffn_router_w").T, "router_b": of("L0_ffn_router_b"),
        "expert_w": np.transpose(of("L0_ffn_expert_w"), (2, 0, 1)).reshape(D, E * D),
        "expert_b": of("L0_ffn_expert_b"),
    }
    arrays = {}

    def feed(group):
        aps = {}
        for name, a in group.items():
            a = np.ascontiguousarray(a)
            arrays[name + "_dram"] = a
            aps[name] = nc.dram_tensor(name + "_dram", a.shape, mybir.dt.from_np(a.dtype), kind="ExternalInput").ap()
        return aps

    cross, latent = feed(cross), feed(latent)
    out = nc.dram_tensor("out_dram", (B, NQ, D), F32, kind="ExternalOutput").ap()
    perceiver_kernel(nc, cross, latent, out)
    r = run_bass_kernel_spmd(nc, [arrays], core_ids=[0])
    return r.results[0]["out_dram"]
```
